# Optimizing a Trainium2 kernel written in Bass

```python
import numpy as np
import jax
import jax.numpy as jnp

def _softmax(x, axis=-1):
    return jax.nn.softmax(x, axis=axis)

def _gelu(x):
    return jax.nn.gelu(x, approximate=True)

def _silu(x):
    return jax.nn.silu(x)

def _sigmoid(x):
    return jax.nn.sigmoid(x)

def _layernorm(x, axis=-1, eps=1e-05):
    m = jnp.mean(x, axis=axis, keepdims=True)
    v = jnp.var(x, axis=axis, keepdims=True)
    return (x - m) / jnp.sqrt(v + eps)

def _scatter_add(tgt, idx, src, axis=0):
    return tgt.at[idx].add(src)

def _segment_sum(src, seg, n):
    return jax.ops.segment_sum(src, seg, n)
kernel_name = 'mk_adj_preln_d1_adj_r2_d2340b'

def setup_inputs(seed: int=0):
    np.random.seed(seed)
    _w = jnp.asarray

    def _rec_inputs():
        import jax
        import jax.numpy as jnp
        _gk = jax.random.key(seed)
        x = -0.0005207 + 1.001 * jax.random.normal(jax.random.fold_in(_gk, 1), (8192, 128), jnp.float32)
        _a = jax.random.bernoulli(jax.random.fold_in(_gk, 2), 0.000244141, (8192, 8192))
        _a = jnp.logical_or(_a, jnp.swapaxes(_a, -1, -2))
        _a = jnp.logical_or(_a, jnp.eye(8192, dtype=bool))
        _af = _a.astype(jnp.float32)
        _af = _af * jax.random.uniform(jax.random.fold_in(_gk, 3), (8192, 8192), jnp.float32, 0.05, 1)
        adj = _af
        return (x, adj)
    x, adj = _rec_inputs()

    def _L0_gnn_setup():
        import jax, jax.numpy as jnp
        import numpy as np
        N = 4096
        D_IN = 128
        D_OUT = 128
        key = jax.random.key(seed)
        k1, k2, k3 = jax.random.split(key, 3)
        x = jax.random.normal(k1, (N, D_IN), dtype=jnp.float32)
        adj = jax.random.uniform(k2, (N, N), dtype=jnp.float32)
        W = jax.random.normal(k3, (D_OUT, D_IN), dtype=jnp.float32) * (1.0 / np.sqrt(D_IN))
        return {'x': x, 'adj': adj, 'W': W}
    _L0_gnn_all = _L0_gnn_setup()
    _L0_gnn_in = {k: v for k, v in _L0_gnn_all.items() if k in ('W',)}
    del _L0_gnn_all
    return {'x': x, 'adj': adj, 'L0_gnn_W': _L0_gnn_in['W']}

def reference(x, adj, L0_gnn_W):
    import jax
    import jax.numpy as jnp

    def _L0_gnn_ref(x, adj, W):
        import jax, jax.numpy as jnp
        import numpy as np
        N = 4096
        D_IN = 128
        D_OUT = 128
        A_hat = adj + jnp.eye(adj.shape[0], dtype=adj.dtype)
        d_inv_sqrt = jnp.sum(A_hat, axis=1) ** (-0.5)
        A_norm = d_inv_sqrt[:, None] * A_hat * d_inv_sqrt[None, :]
        support = x @ W.T
        out = A_norm @ support
        return jax.nn.relu(out)
    h = jnp.maximum(_layernorm(x, axis=-1), 0.0)
    x = x + _L0_gnn_ref(h, adj, L0_gnn_W)
    return x

_drawn_inputs = setup_inputs


def setup_inputs(seed=0):
    import zlib

    import numpy as np

    out = dict(_drawn_inputs(seed))
    spreads = {}
    factors = {}
    for name, (base, spread) in spreads.items():
        noise = np.random.default_rng([zlib.crc32(name.encode()), seed]).standard_normal(out[name].shape)
        drawn = base * np.exp(spread * noise) if base else spread * noise
        out[name] = jnp.asarray(drawn.astype(out[name].dtype))
    for name, factor in factors.items():
        out[name] = (out[name] * factor).astype(out[name].dtype)
    return out
```

```python
import concourse.bass as bass
from concourse import mybir
from contextlib import ExitStack

F32 = mybir.dt.float32
F32R = mybir.dt.float32r
ALU = mybir.AluOpType
ACT = mybir.ActivationFunctionType
AX = mybir.AxisListType


def gnn_kernel(nc: bass.Bass, x: bass.AP, adj: bass.AP, w: bass.AP, out: bass.AP):
    P = 128
    N, D = x.shape
    G = 512
    NB = N // G
    R = G // P
    NT = N // P
    VU = 4
    GROUPS = NB // VU
    XC = 4
    TX = NT // XC
    EPS = 1e-5
    CHAIN_X = TX + 5
    CHAIN_D = 1 + R

    adj_v = adj.rearrange("(i r p) j -> i p r j", r=R, p=P)
    x_v = x.rearrange("(t p) f -> p t f", p=P)
    out_v = out.rearrange("(t p) f -> p t f", p=P)

    ctx = ExitStack()
    with ctx:
        def sb(name, shape, dt=F32):
            return ctx.enter_context(nc.sbuf_tensor(name, shape, dt))

        def pb(name, shape):
            return ctx.enter_context(nc.psum_tensor(name, shape, F32))

        def sem(name):
            return ctx.enter_context(nc.semaphore(name))

        ident = sb("ident", [P, P])
        w_sb = sb("w_sb", [D, D])
        wT = sb("wT", [D, D])
        support = sb("support", [P, NT, D])
        acc = sb("acc", [D, N])
        col = [sb(f"col{i}", [P, R, G]) for i in range(VU)]
        row = [sb(f"row{i}", [P, R, G]) for i in range(VU)]
        hi = [sb(f"hi{i}", [P, 2 * G], F32R) for i in range(4)]
        lo = [sb(f"lo{i}", [P, 2 * G], F32R) for i in range(4)]
        s_hi = [sb(f"s_hi{i}", [P, R, D], F32R) for i in range(2)]
        s_lo = [sb(f"s_lo{i}", [P, R, D], F32R) for i in range(2)]
        part = sb("part", [P, NT, NB])
        total = sb("total", [P, R])
        power = sb("power", [P, TX])
        root = sb("root", [P, R])
        dinv = sb("dinv", [P, NT])
        stats = sb("stats", [P, NT, 6])
        mean2 = sb("mean2", [P, NT])
        gap = sb("gap", [P, NT])
        var = sb("var", [P, NT])
        rstd = sb("rstd", [P, NT])
        shift = sb("shift", [P, NT])
        h = [sb(f"h{i}", [P, R, D]) for i in range(2)]
        hT = [sb(f"hT{i}", [D, R * P]) for i in range(2)]
        unread = [h[0].rearrange("p r d -> p (r d)"), h[1].rearrange("p r d -> p (r d)"), hT[0], hT[1]]
        fin = [sb(f"fin{i}", [D, G]) for i in range(2)]
        y = [sb(f"y{i}", [P, R, D]) for i in range(2)]
        xin = [sb(f"xin{i}", [P, R, D]) for i in range(2)]
        o = [sb(f"o{i}", [P, R, D]) for i in range(2)]

        tp = [pb(f"tp{i}", [P, 2 * G]) for i in range(2)]
        prod = [pb(f"prod{i}", [P, G]) for i in range(2)]
        pre = [pb(f"pre{i}", [P, G]) for i in range(2)]

        ld_w, ident_ok, wT_ps, wT_ok = sem("ld_w"), sem("ident_ok"), sem("wT_ps"), sem("wT_ok")
        ld_x = [sem(f"ld_x{i}") for i in range(XC)]
        ld_col = [sem(f"ld_col{i}") for i in range(VU)]
        ld_row = [sem(f"ld_row{i}") for i in range(VU)]
        stats_chain, stats_ok = sem("stats_chain"), sem("stats_ok")
        var_ok, rstd_ok, total_ok, root_ok = sem("var_ok"), sem("rstd_ok"), sem("total_ok"), sem("root_ok")
        h_ok, hT_ps, hT_ok, sup_ps, sup_ok = sem("h_ok"), sem("hT_ps"), sem("hT_ok"), sem("sup_ps"), sem("sup_ok")
        row_done = sem("row_done")
        tp_done, hi_done, lo_done = sem("tp_done"), sem("hi_done"), sem("lo_done")
        used = sem("used")
        bank_free = sem("bank_free")
        degree_chain, s_ready = sem("degree_chain"), sem("s_ready")
        fin_ok, back_done, t_ok, y_ok, o_ok = sem("fin_ok"), sem("back_done"), sem("t_ok"), sem("y_ok"), sem("o_ok")
        ld_xin = [sem(f"ld_xin{i}") for i in range(2)]
        st_out = [sem(f"st_out{i}") for i in range(2)]

        passed = {e: sem(f"passed_{e}") for e in ("sp", "act", "dve", "pool")}

        block = ctx.enter_context(nc.Block())

        def stand(eng, name):
            eng.sem_inc(passed[name], 1)

        def later(k, g, c, ahead):
            g, c = g + (c + ahead) // VU, (c + ahead) % VU
            return (k + 1, g - GROUPS, c) if isinstance(g, int) and g >= GROUPS else (k, g, c)

        def target(k, g, c):
            return (k + 1 + g * VU + c) & (NB - 1)

        def within(value, least, most):
            return value if isinstance(value, int) else value.with_bounds(min_val=least, max_val=most)

        def either(eng, a, b, then, otherwise):
            if isinstance(b, int) and (b <= 0 or isinstance(a, int)):
                if b > 0 and a < b:
                    then()
                elif otherwise is not None:
                    otherwise()
                return
            with eng.If(a < b):
                then()
            if otherwise is not None:
                with eng.Else():
                    otherwise()

        def groups(eng, body):
            with eng.Fori(0, NB // 2 - 1) as k2:
                for par in range(2):
                    k = k2 * 2 + par
                    with eng.Fori(0, GROUPS - 1) as g:
                        body(k, par, g, False, False)
                    body(k, par, GROUPS - 1, True, False)
            for par in range(2):
                k = NB - 2 + par
                with eng.Fori(0, GROUPS - 1) as g:
                    body(k, par, g, False, False)
                body(k, par, GROUPS - 1, True, par == 1)

        @block.sync
        def _(sp):
            def load_row(i, j, c):
                sp.dma_start(row[c][:], adj_v[bass.ds(i, 1), :, :, bass.ds(j * G, G)]
                             .rearrange("a p r c -> (a p) r c")).then_inc(ld_row[c], 16)

            def load_col(k, g, c):
                i = target(k, g, c)
                sp.dma_start(col[c][:], adj_v[bass.ds(i, 1), :, :, bass.ds(k * G, G)]
                             .rearrange("a p r c -> (a p) r c")).then_inc(ld_col[c], 16)

            sp.dma_start(w_sb[:], w).then_inc(ld_w, 16)
            assert XC == VU
            for q in range(XC):
                sp.dma_start(support[:, q * TX:(q + 1) * TX, :], x_v[:, q * TX:(q + 1) * TX, :]).then_inc(ld_x[q], 16)
                load_row(0, q, q)
            with sp.Fori(1, GROUPS) as g:
                for c in range(VU):
                    sp.wait_ge(row_done, (g - 1) * VU + c + 1)
                    stand(sp, "sp")
                    load_row(0, g * VU + c, c)
            for c in range(VU):
                load_col(0, 0, c)
                sp.wait_ge(row_done, NB - VU + c + 1)
                load_row(1, 1 + c, c)

            def body(k, par, g, step_end, end):
                for c in range(VU):
                    v = k * NB + g * VU + c
                    if not end:
                        sp.wait_ge(lo_done, 2 * v + 2)
                        stand(sp, "sp")
                        load_col(*later(k, g, c, VU))
                        kr, gr, _ = later(k, g, c, VU)
                        j = gr * VU + c
                        sp.wait_ge(row_done, v + NB + 1)
                        stand(sp, "sp")
                        either(sp, j, NB - 1 - kr,
                               lambda: load_row(within(kr + 1, 1, NB - 1), within(kr + 1 + j, 1, NB - 1), c),
                               lambda: sp.sem_inc(ld_row[c], 16))

            groups(sp, body)

            def load_xin(i, c):
                sp.dma_start(xin[c][:], x_v[:, bass.ds(i * R, R), :]).then_inc(ld_xin[c], 16)

            load_xin(0, 0)
            load_xin(1, 1)
            with sp.Fori(0, NB // 2 - 1) as m:
                for c in range(2):
                    i = 2 * m + c
                    sp.wait_ge(o_ok, i + 1)
                    stand(sp, "sp")
                    sp.dma_start(out_v[:, bass.ds(i * R, R), :], o[c][:]).then_inc(st_out[c], 16)
                    load_xin(i + 2, c)
            for c in range(2):
                i = NB - 2 + c
                sp.wait_ge(o_ok, i + 1)
                sp.dma_start(out_v[:, i * R:(i + 1) * R, :], o[c][:]).then_inc(st_out[c], 16)
            for c in range(2):
                sp.wait_ge(st_out[c], 16 * NB // 2)

        @block.gpsimd
        def _(pool):
            nc.gpsimd.memset(ident[:], 0.0).then_inc(ident_ok, 1)
            pool.wait_ge(ident_ok, 1)
            nc.gpsimd.affine_select(out=ident[:], in_=ident[:], compare_op=ALU.not_equal, fill=1.0, base=0,
                                    pattern=[[-1, P]], channel_multiplier=1).then_inc(ident_ok, 1)
            nc.gpsimd.memset(power[:], -0.5).then_inc(ident_ok, 1)
            pool.wait_ge(ident_ok, 3)
            for q in range(XC):
                pool.wait_ge(var_ok, q + 1)
                ts = slice(q * TX, (q + 1) * TX)
                nc.gpsimd.tensor_tensor(rstd[:, ts], var[:, ts], power[:], ALU.pow).then_inc(rstd_ok, 1)
            with pool.Fori(0, NB) as k:
                pool.wait_ge(total_ok, k + 1)
                stand(pool, "pool")
                nc.gpsimd.tensor_tensor(root[:], total[:], power[:, :R], ALU.pow).then_inc(root_ok, 1)
            pool.wait_ge(bank_free, 2 + NB * NB)
            for c in range(2):
                nc.gpsimd.tensor_copy(fin[c][:], acc[:, c * G:(c + 1) * G]).then_inc(fin_ok, 1)
            with pool.Fori(1, NB // 2) as m:
                for c in range(2):
                    pool.wait_ge(t_ok, 2 * m + c - 1)
                    nc.gpsimd.tensor_copy(fin[c][:], acc[:, bass.ds((2 * m + c) * G, G)]).then_inc(fin_ok, 1)

        @block.tensor
        def _(pe):
            pe.sem_inc(used, 4)
            pe.wait_ge(ident_ok, 2)
            pe.wait_ge(ld_w, 16)
            nc.tensor.transpose(prod[0][:, :D], w_sb[:], ident[:]).then_inc(wT_ps, 1)

            def h_transpose(b, c):
                pe.wait_ge(h_ok, R * (b + 1))
                for r in range(R):
                    ins = nc.tensor.transpose(pre[0][:, r * P:(r + 1) * P], h[c][:, r, :], ident[:])
                ins.then_inc(hT_ps, 1)

            def h_product(b, c):
                pe.wait_ge(hT_ok, b + 1)
                for r in range(R):
                    ins = nc.tensor.matmul(pre[1][:, r * D:(r + 1) * D], hT[c][:, r * P:(r + 1) * P], wT[:],
                                           start=True, stop=True)
                ins.then_inc(sup_ps, 1)

            pe.wait_ge(wT_ok, 1)
            h_transpose(0, 0)
            h_product(0, 0)
            h_transpose(1, 1)
            with pe.Fori(0, NB // 2 - 1) as m:
                for c in (1, 0):
                    b = 2 * m + 2 - c
                    pe.wait_ge(sup_ok, b)
                    h_product(b, c)
                    h_transpose(b + 1, 1 - c)
            pe.wait_ge(sup_ok, NB - 1)
            h_product(NB - 1, 1)

            def transposes(k, g, c, half):
                if half == 0:
                    pe.wait_ge(ld_col[c], 16 * (k * GROUPS + g + 1))
                for jj in range(2):
                    j = 2 * half + jj
                    for r in range(R):
                        ins = nc.tensor.transpose(tp[half][:, jj * G + r * P:jj * G + (r + 1) * P],
                                                  col[c][:, r, j * P:(j + 1) * P], ident[:])
                ins.then_inc(tp_done, 1)

            transposes(0, 0, 0, 0)
            transposes(0, 0, 0, 1)

            def body(k, par, g, step_end, end):
                for c in range(VU):
                    v = k * NB + g * VU + c
                    for half in range(2):
                        pe.wait_ge(lo_done, 2 * v + half + 1)
                        if not (end and c == VU - 1):
                            transposes(*later(k, g, c, 1), half)
                        if half == 0:
                            pe.wait_ge(bank_free, v + 1)
                            if c == 0:
                                pe.wait_ge(s_ready, k + 1)
                        a = (2 * c + half) % 4
                        for jj in range(2):
                            j = 2 * half + jj
                            at = slice(jj * G, (jj + 1) * G)
                            for n, (s, m) in enumerate(((s_hi, hi), (s_lo, hi), (s_hi, lo))):
                                ins = nc.tensor.matmul(prod[c % 2][:], s[par][:, j, :], m[a][:, at],
                                                       start=(j == 0 and n == 0), stop=(j == R - 1 and n == 2))
                        ins.then_inc(used, 1)

            groups(pe, body)

            with pe.Fori(0, NB // 2) as m:
                for c in range(2):
                    pe.wait_ge(fin_ok, 2 * m + c + 1)
                    for r in range(R):
                        ins = nc.tensor.transpose(prod[c][:, r * D:(r + 1) * D], fin[c][:, r * P:(r + 1) * P], ident[:])
                    ins.then_inc(back_done, 1)

        @block.scalar
        def _(act):
            def row_sums(i, j, c):
                for r in range(R):
                    ins = nc.scalar.activation(row[c][:, r, :], row[c][:, r, :], ACT.Copy,
                                               accum_out=part[:, bass.ds(i * R + r, 1), bass.ds(j, 1)]
                                               .rearrange("p a b -> p (a b)"))
                return ins

            def layernorm(b, c):
                act.wait_ge(stats_ok, b // (TX // R) + 1)
                for r in range(R):
                    t = b * R + r
                    nc.scalar.activation(h[c][:, r, :], support[:, bass.ds(t, 1), :].rearrange("p a f -> p (a f)"),
                                         ACT.Relu, bias=shift[:, bass.ds(t, 1)],
                                         scale=rstd[:, bass.ds(t, 1)]).then_inc(h_ok, 1)

            def first_sums(g, c):
                act.wait_ge(ld_row[c], 16 * (g + 1))
                row_sums(0, g * VU + c, c).then_inc(row_done, 1)

            for c in range(VU):
                if c >= 2:
                    act.wait_ge(hT_ps, c - 1)
                layernorm(c, c % 2)
                first_sums(0, c)
            with act.Fori(1, GROUPS) as g:
                for c in range(VU):
                    act.wait_ge(hT_ps, g * VU + c - 1)
                    layernorm(g * VU + c, c % 2)
                    first_sums(g, c)

            def block_sums(k, g, c):
                i = target(k, g, c)
                act.wait_ge(ld_col[c], 16 * (k * GROUPS + g + 1))
                stand(act, "act")

                def sums():
                    for r in range(R // 2, R):
                        nc.scalar.activation(unread[c % 2 * 2 + r - R // 2][:], col[c][:, r, :], ACT.Copy,
                                             accum_out=part[:, bass.ds(i * R + r, 1), bass.ds(k, 1)]
                                             .rearrange("p a b -> p (a b)"))

                either(act, g * VU + c, NB - 1 - k, sums, None)

            act.wait_ge(sup_ps, NB)
            def body(k, par, g, step_end, end):
                for c in range(VU):
                    s = g * VU + c
                    v = k * NB + s
                    for half in range(2):
                        q = 2 * v + half
                        act.wait_ge(used, q + 1)
                        act.wait_ge(tp_done, q + 1)
                        nc.scalar.activation(hi[(2 * c + half) % 4][:], tp[half][:], ACT.Copy).then_inc(hi_done, 1)
                        if half == 0:
                            block_sums(k, g, c)
                    act.wait_ge(ld_row[c], 16 * (GROUPS * (k + 1) + g + 1))
                    stand(act, "act")
                    either(act, s, NB - 1 - k,
                           lambda: row_sums(within(k + 1, 1, NB - 1), within(k + 1 + s, 1, NB - 1), c)
                           .then_inc(row_done, 1),
                           lambda: nc.scalar.activation(row[c][:, 0, 0:1], row[c][:, 0, 0:1], ACT.Copy)
                           .then_inc(row_done, 1))

            groups(act, body)

            with act.Fori(0, NB // 2) as m:
                for c in range(2):
                    i = 2 * m + c
                    act.wait_ge(t_ok, i + 1)
                    for r in range(R):
                        ins = nc.scalar.activation(y[c][:, r, :], y[c][:, r, :], ACT.Relu,
                                                   scale=dinv[:, bass.ds(i * R + r, 1)])
                    ins.then_inc(y_ok, 1)

        @block.vector
        def _(dve):
            for n in range(2):
                nc.vector.memset(acc[:, n * (N // 2):(n + 1) * (N // 2)], 0.0).then_inc(bank_free, 1)
            dve.wait_ge(wT_ps, 1)
            nc.vector.tensor_copy(wT[:], prod[0][:, :D]).then_inc(wT_ok, 1)
            for q in range(XC):
                dve.wait_ge(ld_x[q], 16)
                done = q * CHAIN_X
                with dve.Fori(q * TX, (q + 1) * TX) as t:
                    nc.vector.bn_stats(stats[:, bass.ds(t, 1), :].rearrange("p a s -> p (a s)"),
                                       support[:, bass.ds(t, 1), :].rearrange("p a f -> p (a f)")).then_inc(stats_chain, 1)
                dve.wait_ge(stats_chain, done + TX)
                ts = slice(q * TX, (q + 1) * TX)
                even, odd = stats[:, ts, 0:3], stats[:, ts, 3:6]
                nc.vector.tensor_tensor(mean2[:, ts], even[:, :, 1], odd[:, :, 1], ALU.add).then_inc(stats_chain, 1)
                nc.vector.tensor_tensor(gap[:, ts], even[:, :, 1], odd[:, :, 1], ALU.subtract).then_inc(stats_chain, 1)
                nc.vector.tensor_tensor(var[:, ts], even[:, :, 2], odd[:, :, 2], ALU.add).then_inc(stats_chain, 1)
                dve.wait_ge(stats_chain, done + TX + 2)
                nc.vector.scalar_tensor_tensor(out=gap[:, ts], in0=gap[:, ts], scalar=D / 4, in1=gap[:, ts],
                                               op0=ALU.mult, op1=ALU.mult).then_inc(stats_chain, 1)
                dve.wait_ge(stats_chain, done + TX + 4)
                nc.vector.tensor_tensor(var[:, ts], var[:, ts], gap[:, ts], ALU.add).then_inc(stats_chain, 1)
                dve.wait_ge(stats_chain, done + CHAIN_X)
                nc.vector.tensor_scalar(var[:, ts], var[:, ts], 1 / D, EPS, ALU.mult, ALU.add).then_inc(var_ok, 1)
                dve.wait_ge(rstd_ok, q + 1)
                nc.vector.scalar_tensor_tensor(out=shift[:, ts], in0=mean2[:, ts], scalar=-0.5, in1=rstd[:, ts],
                                               op0=ALU.mult, op1=ALU.mult).then_inc(stats_ok, 1)

            def hT_out(b, c):
                dve.wait_ge(hT_ps, b + 1)
                nc.vector.tensor_copy(hT[c][:], pre[0][:]).then_inc(hT_ok, 1)

            def support_out(b):
                dve.wait_ge(sup_ps, b + 1)
                nc.vector.tensor_copy(support[:, bass.ds(b * R, R), :].rearrange("p a f -> p (a f)"),
                                      pre[1][:]).then_inc(sup_ok, 1)

            hT_out(0, 0)
            with dve.Fori(0, NB // 2 - 1) as m:
                for c in (1, 0):
                    b = 2 * m + 2 - c
                    hT_out(b, c)
                    support_out(b - 1)
            hT_out(NB - 1, 1)
            support_out(NB - 2)
            support_out(NB - 1)

            def scale_support(i, par):
                done = i * CHAIN_D
                nc.vector.tensor_reduce(total[:], part[:, bass.ds(i * R, R), :], AX.X, ALU.add).then_inc(degree_chain, 1)
                dve.wait_ge(degree_chain, done + 1)
                nc.vector.tensor_scalar(total[:], total[:], 1.0, None, ALU.add).then_inc(total_ok, 1)
                dve.wait_ge(root_ok, i + 1)
                nc.vector.tensor_copy(dinv[:, bass.ds(i * R, R)], root[:])
                for r in range(R):
                    nc.vector.tensor_scalar(s_hi[par][:, r, :],
                                            support[:, bass.ds(i * R + r, 1), :].rearrange("p a f -> p (a f)"),
                                            root[:, r:r + 1], None, ALU.mult).then_inc(degree_chain, 1)
                for r in range(R):
                    dve.wait_ge(degree_chain, done + 2 + r)
                    ins = nc.vector.scalar_tensor_tensor(
                        out=s_lo[par][:, r, :],
                        in0=support[:, bass.ds(i * R + r, 1), :].rearrange("p a f -> p (a f)"),
                        scalar=root[:, r:r + 1], in1=s_hi[par][:, r, :].bitcast(F32),
                        op0=ALU.mult, op1=ALU.subtract)
                ins.then_inc(s_ready, 1)

            def block_sums(k, g, c):
                i = target(k, g, c)
                dve.wait_ge(ld_col[c], 16 * (k * GROUPS + g + 1))
                stand(dve, "dve")
                either(dve, g * VU + c, NB - 1 - k, lambda: nc.vector.tensor_reduce(
                    part[:, bass.ds(i * R, R // 2), bass.ds(k, 1)].rearrange("p r a -> p (r a)"),
                    col[c][:, 0:R // 2, :], AX.X, ALU.add), None)

            def remainder(k, g, c, half):
                dve.wait_ge(hi_done, 2 * (k * NB + g * VU + c) + half + 1)
                a = (2 * c + half) % 4
                nc.vector.tensor_tensor(lo[a][:], tp[half][:], hi[a][:].bitcast(F32), ALU.subtract).then_inc(lo_done, 1)

            dve.wait_ge(row_done, NB)
            scale_support(0, 0)
            remainder(0, 0, 0, 0)
            block_sums(0, 0, 0)
            remainder(0, 0, 0, 1)

            def body(k, par, g, step_end, end):
                for c in range(VU):
                    v = k * NB + g * VU + c
                    if step_end and not end and c == VU - 1:
                        dve.wait_ge(row_done, (NB - 1) * k + 2 * NB - 1)
                        scale_support(k + 1, 1 - par)
                    if not (end and c == VU - 1):
                        following = later(k, g, c, 1)
                        remainder(*following, 0)
                        block_sums(*following)
                        remainder(*following, 1)
                    i = target(k, g, c)
                    dve.wait_ge(used, 4 + 2 * v + 2)
                    nc.vector.tensor_tensor(acc[:, bass.ds(i * G, G)], prod[c % 2][:], acc[:, bass.ds(i * G, G)],
                                            ALU.add).then_inc(bank_free, 1)

            groups(dve, body)

            def result(m, c):
                i = 2 * m + c
                dve.wait_ge(back_done, i + 1)
                for r in range(R):
                    t = i * R + r
                    ins = nc.vector.scalar_tensor_tensor(
                        out=y[c][:, r, :], in0=support[:, bass.ds(t, 1), :].rearrange("p a f -> p (a f)"),
                        scalar=dinv[:, bass.ds(t, 1)], in1=prod[c][:, r * D:(r + 1) * D],
                        op0=ALU.mult, op1=ALU.add)
                ins.then_inc(t_ok, 1)
                dve.wait_ge(y_ok, i + 1)
                dve.wait_ge(ld_xin[c], 16 * (m + 1))
                if not isinstance(m, int):
                    dve.wait_ge(st_out[c], 16 * m)
                nc.vector.tensor_tensor(o[c][:], y[c][:], xin[c][:], ALU.add).then_inc(o_ok, 1)

            for c in range(2):
                result(0, c)
            with dve.Fori(1, NB // 2) as m:
                for c in range(2):
                    result(m, c)


_INS = ['x', 'adj', 'L0_gnn_W']
_OUTS = [((8192, 128), 'float32')]


def kernel(**inputs):
    import numpy as _np
    import concourse.bacc as _bacc
    from concourse import mybir as _mybir
    from concourse.bass_utils import run_bass_kernel_spmd as _run

    nc = _bacc.Bacc("TRN2", target_bir_lowering=False, num_devices=1)
    arrays, args = {}, []
    for name in _INS:
        a = _np.ascontiguousarray(inputs[name])
        arrays[f"in_{name}_dram"] = a
        args.append(nc.dram_tensor(f"in_{name}_dram", a.shape, _mybir.dt.from_np(a.dtype), kind="ExternalInput").ap())
    for i, (shape, dtype) in enumerate(_OUTS):
        dt = _mybir.dt.from_np(_np.dtype(dtype))
        args.append(nc.dram_tensor(f"out_{i}_dram", shape, dt, kind="ExternalOutput").ap())
    gnn_kernel(nc, *args)
    r = _run(nc, [arrays], core_ids=[0])
    got = tuple(r.results[0][f"out_{i}_dram"] for i in range(len(_OUTS)))
    return got[0]
```

```python
import concourse.bass as bass
from concourse import mybir
from contextlib import ExitStack

F32 = mybir.dt.float32
F32R = mybir.dt.float32r
ALU = mybir.AluOpType
ACT = mybir.ActivationFunctionType
AX = mybir.AxisListType


def gnn_kernel(nc: bass.Bass, x: bass.AP, adj: bass.AP, w: bass.AP, out: bass.AP):
    P = 128
    N, D = x.shape
    G = 512
    NB = N // G
    R = G // P
    NT = N // P
    VU = 4
    GROUPS = NB // VU
    XC = 4
    TX = NT // XC
    EPS = 1e-5
    CHAIN_X = TX + 5
    CHAIN_D = 1 + R

    adj_v = adj.rearrange("(i r p) j -> i p r j", r=R, p=P)
    x_v = x.rearrange("(t p) f -> p t f", p=P)
    out_v = out.rearrange("(t p) f -> p t f", p=P)

    ctx = ExitStack()
    with ctx:
        def sb(name, shape, dt=F32):
            return ctx.enter_context(nc.sbuf_tensor(name, shape, dt))

        def pb(name, shape):
            return ctx.enter_context(nc.psum_tensor(name, shape, F32))

        def sem(name):
            return ctx.enter_context(nc.semaphore(name))

        ident = sb("ident", [P, P])
        w_sb = sb("w_sb", [D, D])
        wT = sb("wT", [D, D])
        support = sb("support", [P, NT, D])
        acc = sb("acc", [D, N])
        col = [sb(f"col{i}", [P, R, G]) for i in range(VU)]
        row = [sb(f"row{i}", [P, R, G]) for i in range(VU)]
        hi = [sb(f"hi{i}", [P, 2 * G], F32R) for i in range(4)]
        lo = [sb(f"lo{i}", [P, 2 * G], F32R) for i in range(4)]
        s_hi = [sb(f"s_hi{i}", [P, R, D], F32R) for i in range(2)]
        s_lo = [sb(f"s_lo{i}", [P, R, D], F32R) for i in range(2)]
        part = sb("part", [P, NT, NB])
        total = sb("total", [P, R])
        power = sb("power", [P, TX])
        root = sb("root", [P, R])
        dinv = sb("dinv", [P, NT])
        stats = sb("stats", [P, NT, 6])
        mean2 = sb("mean2", [P, NT])
        gap = sb("gap", [P, NT])
        var = sb("var", [P, NT])
        rstd = sb("rstd", [P, NT])
        shift = sb("shift", [P, NT])
        h = [sb(f"h{i}", [P, R, D]) for i in range(2)]
        hT = [sb(f"hT{i}", [D, R * P]) for i in range(2)]
        unread = [h[0].rearrange("p r d -> p (r d)"), h[1].rearrange("p r d -> p (r d)"), hT[0], hT[1]]
        fin = [sb(f"fin{i}", [D, G]) for i in range(2)]
        y = [sb(f"y{i}", [P, R, D]) for i in range(2)]
        xin = [sb(f"xin{i}", [P, R, D]) for i in range(2)]
        o = [sb(f"o{i}", [P, R, D]) for i in range(2)]

        tp = [pb(f"tp{i}", [P, 2 * G]) for i in range(2)]
        prod = [pb(f"prod{i}", [P, G]) for i in range(2)]
        pre = [pb(f"pre{i}", [P, G]) for i in range(2)]

        ld_w, ident_ok, wT_ps, wT_ok = sem("ld_w"), sem("ident_ok"), sem("wT_ps"), sem("wT_ok")
        ld_x = [sem(f"ld_x{i}") for i in range(XC)]
        ld_col = [sem(f"ld_col{i}") for i in range(VU)]
        ld_row = [sem(f"ld_row{i}") for i in range(VU)]
        stats_chain, stats_ok = sem("stats_chain"), sem("stats_ok")
        var_ok, rstd_ok, total_ok, root_ok = sem("var_ok"), sem("rstd_ok"), sem("total_ok"), sem("root_ok")
        h_ok, hT_ps, hT_ok, sup_ps, sup_ok = sem("h_ok"), sem("hT_ps"), sem("hT_ok"), sem("sup_ps"), sem("sup_ok")
        row_done = sem("row_done")
        tp_done, hi_done, lo_done = sem("tp_done"), sem("hi_done"), sem("lo_done")
        used = sem("used")
        bank_free = sem("bank_free")
        degree_chain, s_ready = sem("degree_chain"), sem("s_ready")
        fin_ok, back_done, t_ok, y_ok, o_ok = sem("fin_ok"), sem("back_done"), sem("t_ok"), sem("y_ok"), sem("o_ok")
        ld_xin = [sem(f"ld_xin{i}") for i in range(2)]
        st_out = [sem(f"st_out{i}") for i in range(2)]

        passed = {e: sem(f"passed_{e}") for e in ("sp", "act", "dve", "pool")}

        block = ctx.enter_context(nc.Block())

        def stand(eng, name):
            eng.sem_inc(passed[name], 1)

        def later(k, g, c, ahead):
            g, c = g + (c + ahead) // VU, (c + ahead) % VU
            return (k + 1, g - GROUPS, c) if isinstance(g, int) and g >= GROUPS else (k, g, c)

        def is_last(k):
            return isinstance(k, int) and k == NB - 1

        def target(k, g, c):
            return (k + 1 + g * VU + c) & (NB - 1)

        def within(value, least, most):
            return value if isinstance(value, int) else value.with_bounds(min_val=least, max_val=most)

        def either(eng, condition, then, otherwise):
            if isinstance(condition, bool):
                chosen = then if condition else otherwise
                if chosen is not None:
                    chosen()
                return
            with eng.If(condition):
                then()
            if otherwise is not None:
                with eng.Else():
                    otherwise()

        def summed(k, g, c):
            return not is_last(k) and g * VU + c < NB - 1 - k

        def in_row_stream(k, g, c):
            if is_last(k) or (isinstance(g, int) and g * VU + c == NB - 1):
                return False
            return k < ((g * VU + c + 1) & (NB - 1))

        def groups(eng, body):
            with eng.Fori(0, NB // 2 - 1) as k2:
                for par in range(2):
                    k = k2 * 2 + par
                    with eng.Fori(0, GROUPS - 1) as g:
                        body(k, par, g, False)
                    body(k, par, GROUPS - 1, True)
            with eng.Fori(0, GROUPS - 1) as g:
                body(NB - 2, 0, g, False)
            body(NB - 2, 0, GROUPS - 1, True)
            for g in range(GROUPS):
                body(NB - 1, 1, g, g == GROUPS - 1)

        @block.sync
        def _(sp):
            def load_row(i, j, c):
                sp.dma_start(row[c][:], adj_v[bass.ds(i, 1), :, :, bass.ds(j * G, G)]
                             .rearrange("a p r c -> (a p) r c")).then_inc(ld_row[c], 16)

            def load_col(k, g, c):
                i = target(k, g, c)
                sp.dma_start(col[c][:], adj_v[bass.ds(i, 1), :, :, bass.ds(k * G, G)]
                             .rearrange("a p r c -> (a p) r c")).then_inc(ld_col[c], 16)

            sp.dma_start(w_sb[:], w).then_inc(ld_w, 16)
            assert XC == VU
            for q in range(XC):
                sp.dma_start(support[:, q * TX:(q + 1) * TX, :], x_v[:, q * TX:(q + 1) * TX, :]).then_inc(ld_x[q], 16)
                load_row(0, q, q)
            with sp.Fori(1, GROUPS) as g:
                for c in range(VU):
                    sp.wait_ge(row_done, (g - 1) * VU + c + 1)
                    stand(sp, "sp")
                    load_row(0, g * VU + c, c)
            for c in range(VU):
                load_col(0, 0, c)
                sp.wait_ge(row_done, NB - VU + c + 1)
                load_row(1, 1 + c, c)

            def body(k, par, g, step_end):
                end = is_last(k) and step_end
                for c in range(VU):
                    v = k * NB + g * VU + c
                    if not end:
                        sp.wait_ge(lo_done, 2 * v + 2)
                        stand(sp, "sp")
                        load_col(*later(k, g, c, VU))
                        kr, gr, _ = later(k, g, c, VU)
                        if is_last(kr):
                            continue
                        j = gr * VU + c + 1
                        sp.wait_ge(row_done, v + NB + 1)
                        stand(sp, "sp")
                        either(sp, in_row_stream(kr, gr, c),
                               lambda: load_row(within(kr + 1, 1, NB - 1), within(j, 1, NB - 1), c),
                               lambda: sp.sem_inc(ld_row[c], 16))

            groups(sp, body)

        @block.gpsimd
        def _(pool):
            nc.gpsimd.memset(ident[:], 0.0).then_inc(ident_ok, 1)
            pool.wait_ge(ident_ok, 1)
            nc.gpsimd.affine_select(out=ident[:], in_=ident[:], compare_op=ALU.not_equal, fill=1.0, base=0,
                                    pattern=[[-1, P]], channel_multiplier=1).then_inc(ident_ok, 1)
            nc.gpsimd.memset(power[:], -0.5).then_inc(ident_ok, 1)
            pool.wait_ge(ident_ok, 3)
            for q in range(XC):
                pool.wait_ge(var_ok, q + 1)
                ts = slice(q * TX, (q + 1) * TX)
                nc.gpsimd.tensor_tensor(rstd[:, ts], var[:, ts], power[:], ALU.pow).then_inc(rstd_ok, 1)
            with pool.Fori(0, NB) as k:
                pool.wait_ge(total_ok, k + 1)
                stand(pool, "pool")
                nc.gpsimd.tensor_tensor(root[:], total[:], power[:, :R], ALU.pow).then_inc(root_ok, 1)
            def load_xin(i, c):
                pool.dma_start(xin[c][:], x_v[:, bass.ds(i * R, R), :]).then_inc(ld_xin[c], 16)

            def finish(m, c):
                i = 2 * m + c
                pool.wait_ge(ld_xin[c], 16 * (m + 1))
                if not isinstance(m, int):
                    pool.wait_ge(st_out[c], 16 * m)
                pool.wait_ge(y_ok, i + 1)
                nc.gpsimd.tensor_tensor(o[c][:], y[c][:], xin[c][:], ALU.add).then_inc(o_ok, 1)
                pool.wait_ge(o_ok, i + 1)
                stand(pool, "pool")
                pool.dma_start(out_v[:, bass.ds(i * R, R), :], o[c][:]).then_inc(st_out[c], 16)

            for c in range(2):
                load_xin(c, c)
            for c in range(2):
                finish(0, c)
                load_xin(2 + c, c)
            with pool.Fori(1, NB // 2 - 1) as m:
                for c in range(2):
                    finish(m, c)
                    load_xin(2 * m + 2 + c, c)
            m = NB // 2 - 1
            for c in range(2):
                pool.wait_ge(st_out[c], 16 * m)
                finish(m, c)
            for c in range(2):
                pool.wait_ge(st_out[c], 16 * NB // 2)

        @block.tensor
        def _(pe):
            pe.sem_inc(used, 4)
            pe.wait_ge(ident_ok, 2)
            pe.wait_ge(ld_w, 16)
            nc.tensor.transpose(prod[0][:, :D], w_sb[:], ident[:]).then_inc(wT_ps, 1)

            def h_transpose(b, c):
                pe.wait_ge(h_ok, R * (b + 1))
                for r in range(R):
                    ins = nc.tensor.transpose(pre[0][:, r * P:(r + 1) * P], h[c][:, r, :], ident[:])
                ins.then_inc(hT_ps, 1)

            def h_product(b, c):
                pe.wait_ge(hT_ok, b + 1)
                for r in range(R):
                    ins = nc.tensor.matmul(pre[1][:, r * D:(r + 1) * D], hT[c][:, r * P:(r + 1) * P], wT[:],
                                           start=True, stop=True)
                ins.then_inc(sup_ps, 1)

            pe.wait_ge(wT_ok, 1)
            h_transpose(0, 0)
            h_product(0, 0)
            h_transpose(1, 1)
            with pe.Fori(0, NB // 2 - 1) as m:
                for c in (1, 0):
                    b = 2 * m + 2 - c
                    pe.wait_ge(sup_ok, b)
                    h_product(b, c)
                    h_transpose(b + 1, 1 - c)
            pe.wait_ge(sup_ok, NB - 1)
            h_product(NB - 1, 1)

            def transposes(k, g, c, half):
                if half == 0:
                    pe.wait_ge(ld_col[c], 16 * (k * GROUPS + g + 1))
                for jj in range(2):
                    j = 2 * half + jj
                    for r in range(R):
                        ins = nc.tensor.transpose(tp[half][:, jj * G + r * P:jj * G + (r + 1) * P],
                                                  col[c][:, r, j * P:(j + 1) * P], ident[:])
                ins.then_inc(tp_done, 1)

            def rows_back(i):
                c = i % 2
                pe.wait_ge(fin_ok, i + 1)
                if i >= 2:
                    pe.wait_ge(t_ok, i - 1)
                for r in range(R):
                    ins = nc.tensor.transpose(pre[c][:, r * D:(r + 1) * D], fin[c][:, r * P:(r + 1) * P], ident[:])
                ins.then_inc(back_done, 1)

            transposes(0, 0, 0, 0)
            transposes(0, 0, 0, 1)

            def body(k, par, g, step_end):
                end = is_last(k) and step_end
                for c in range(VU):
                    v = k * NB + g * VU + c
                    for half in range(2):
                        pe.wait_ge(lo_done, 2 * v + half + 1)
                        if not (end and c == VU - 1):
                            transposes(*later(k, g, c, 1), half)
                        if half == 0:
                            if is_last(k) and g * VU + c >= 2:
                                pe.wait_ge(fin_ok, g * VU + c - 1)
                            else:
                                pe.wait_ge(bank_free, v + 1)
                            if c == 0:
                                pe.wait_ge(s_ready, k + 1)
                        a = (2 * c + half) % 4
                        for jj in range(2):
                            j = 2 * half + jj
                            at = slice(jj * G, (jj + 1) * G)
                            for n, (s, m) in enumerate(((s_hi, hi), (s_lo, hi), (s_hi, lo))):
                                ins = nc.tensor.matmul(prod[c % 2][:], s[par][:, j, :], m[a][:, at],
                                                       start=(j == 0 and n == 0), stop=(j == R - 1 and n == 2))
                        ins.then_inc(used, 1)
                        if is_last(k) and half == 0 and v > NB * (NB - 1):
                            rows_back(g * VU + c - 1)

            groups(pe, body)

            rows_back(NB - 1)

        @block.scalar
        def _(act):
            def row_sums(i, j, c):
                for r in range(R):
                    ins = nc.scalar.activation(row[c][:, r, :], row[c][:, r, :], ACT.Copy,
                                               accum_out=part[:, bass.ds(i * R + r, 1), bass.ds(j, 1)]
                                               .rearrange("p a b -> p (a b)"))
                return ins

            def layernorm(b, c):
                act.wait_ge(stats_ok, b // (TX // R) + 1)
                for r in range(R):
                    t = b * R + r
                    nc.scalar.activation(h[c][:, r, :], support[:, bass.ds(t, 1), :].rearrange("p a f -> p (a f)"),
                                         ACT.Relu, bias=shift[:, bass.ds(t, 1)],
                                         scale=rstd[:, bass.ds(t, 1)]).then_inc(h_ok, 1)

            def first_sums(g, c):
                act.wait_ge(ld_row[c], 16 * (g + 1))
                row_sums(0, g * VU + c, c).then_inc(row_done, 1)

            for c in range(VU):
                if c >= 2:
                    act.wait_ge(hT_ps, c - 1)
                layernorm(c, c % 2)
                first_sums(0, c)
            with act.Fori(1, GROUPS) as g:
                for c in range(VU):
                    act.wait_ge(hT_ps, g * VU + c - 1)
                    layernorm(g * VU + c, c % 2)
                    first_sums(g, c)

            def block_sums(k, g, c):
                i = target(k, g, c)
                act.wait_ge(ld_col[c], 16 * (k * GROUPS + g + 1))
                stand(act, "act")

                def sums():
                    for r in range(R // 2, R):
                        nc.scalar.activation(unread[c % 2 * 2 + r - R // 2][:], col[c][:, r, :], ACT.Copy,
                                             accum_out=part[:, bass.ds(i * R + r, 1), bass.ds(k, 1)]
                                             .rearrange("p a b -> p (a b)"))

                either(act, summed(k, g, c), sums, None)

            def relu(i):
                act.wait_ge(t_ok, i + 1)
                for r in range(R):
                    ins = nc.scalar.activation(y[i % 2][:, r, :], y[i % 2][:, r, :], ACT.Relu,
                                               scale=dinv[:, i * R + r:i * R + r + 1])
                ins.then_inc(y_ok, 1)

            act.wait_ge(sup_ps, NB)

            def body(k, par, g, step_end):
                end = is_last(k) and step_end
                for c in range(VU):
                    s = g * VU + c
                    v = k * NB + s
                    for half in range(2):
                        q = 2 * v + half
                        act.wait_ge(used, q + 1)
                        act.wait_ge(tp_done, q + 1)
                        nc.scalar.activation(hi[(2 * c + half) % 4][:], tp[half][:], ACT.Copy).then_inc(hi_done, 1)
                        if half == 0:
                            block_sums(k, g, c)
                    if is_last(k):
                        if s >= 3:
                            relu(s - 3)
                        continue
                    act.wait_ge(ld_row[c], 16 * (GROUPS * (k + 1) + g + 1))
                    stand(act, "act")
                    either(act, in_row_stream(k, g, c),
                           lambda: row_sums(within(k + 1, 1, NB - 1), within(s + 1, 1, NB - 1), c)
                           .then_inc(row_done, 1),
                           lambda: nc.scalar.activation(row[c][:, 0, 0:1], row[c][:, 0, 0:1], ACT.Copy)
                           .then_inc(row_done, 1))

            groups(act, body)

            for i in range(NB - 3, NB):
                relu(i)

        @block.vector
        def _(dve):
            for n in range(2):
                nc.vector.memset(acc[:, n * (N // 2):(n + 1) * (N // 2)], 0.0).then_inc(bank_free, 1)
            dve.wait_ge(wT_ps, 1)
            nc.vector.tensor_copy(wT[:], prod[0][:, :D]).then_inc(wT_ok, 1)
            for q in range(XC):
                dve.wait_ge(ld_x[q], 16)
                done = q * CHAIN_X
                with dve.Fori(q * TX, (q + 1) * TX) as t:
                    nc.vector.bn_stats(stats[:, bass.ds(t, 1), :].rearrange("p a s -> p (a s)"),
                                       support[:, bass.ds(t, 1), :].rearrange("p a f -> p (a f)")).then_inc(stats_chain, 1)
                dve.wait_ge(stats_chain, done + TX)
                ts = slice(q * TX, (q + 1) * TX)
                even, odd = stats[:, ts, 0:3], stats[:, ts, 3:6]
                nc.vector.tensor_tensor(mean2[:, ts], even[:, :, 1], odd[:, :, 1], ALU.add).then_inc(stats_chain, 1)
                nc.vector.tensor_tensor(gap[:, ts], even[:, :, 1], odd[:, :, 1], ALU.subtract).then_inc(stats_chain, 1)
                nc.vector.tensor_tensor(var[:, ts], even[:, :, 2], odd[:, :, 2], ALU.add).then_inc(stats_chain, 1)
                dve.wait_ge(stats_chain, done + TX + 2)
                nc.vector.scalar_tensor_tensor(out=gap[:, ts], in0=gap[:, ts], scalar=D / 4, in1=gap[:, ts],
                                               op0=ALU.mult, op1=ALU.mult).then_inc(stats_chain, 1)
                dve.wait_ge(stats_chain, done + TX + 4)
                nc.vector.tensor_tensor(var[:, ts], var[:, ts], gap[:, ts], ALU.add).then_inc(stats_chain, 1)
                dve.wait_ge(stats_chain, done + CHAIN_X)
                nc.vector.tensor_scalar(var[:, ts], var[:, ts], 1 / D, EPS, ALU.mult, ALU.add).then_inc(var_ok, 1)
                dve.wait_ge(rstd_ok, q + 1)
                nc.vector.scalar_tensor_tensor(out=shift[:, ts], in0=mean2[:, ts], scalar=-0.5, in1=rstd[:, ts],
                                               op0=ALU.mult, op1=ALU.mult).then_inc(stats_ok, 1)

            def hT_out(b, c):
                dve.wait_ge(hT_ps, b + 1)
                nc.vector.tensor_copy(hT[c][:], pre[0][:]).then_inc(hT_ok, 1)

            def support_out(b):
                dve.wait_ge(sup_ps, b + 1)
                nc.vector.tensor_copy(support[:, bass.ds(b * R, R), :].rearrange("p a f -> p (a f)"),
                                      pre[1][:]).then_inc(sup_ok, 1)

            hT_out(0, 0)
            with dve.Fori(0, NB // 2 - 1) as m:
                for c in (1, 0):
                    b = 2 * m + 2 - c
                    hT_out(b, c)
                    support_out(b - 1)
            hT_out(NB - 1, 1)
            support_out(NB - 2)
            support_out(NB - 1)

            def add_totals(i):
                nc.vector.tensor_reduce(total[:], part[:, bass.ds(i * R, R), :], AX.X, ALU.add).then_inc(degree_chain, 1)
                dve.wait_ge(degree_chain, i * CHAIN_D + 1)
                nc.vector.tensor_scalar(total[:], total[:], 1.0, None, ALU.add).then_inc(total_ok, 1)

            def scale_support(i, par):
                dve.wait_ge(root_ok, i + 1)
                nc.vector.tensor_copy(dinv[:, bass.ds(i * R, R)], root[:])
                for r in range(R):
                    nc.vector.tensor_scalar(s_hi[par][:, r, :],
                                            support[:, bass.ds(i * R + r, 1), :].rearrange("p a f -> p (a f)"),
                                            root[:, r:r + 1], None, ALU.mult).then_inc(degree_chain, 1)
                for r in range(R):
                    dve.wait_ge(degree_chain, i * CHAIN_D + 2 + r)
                    ins = nc.vector.scalar_tensor_tensor(
                        out=s_lo[par][:, r, :],
                        in0=support[:, bass.ds(i * R + r, 1), :].rearrange("p a f -> p (a f)"),
                        scalar=root[:, r:r + 1], in1=s_hi[par][:, r, :].bitcast(F32),
                        op0=ALU.mult, op1=ALU.subtract)
                ins.then_inc(s_ready, 1)

            def block_sums(k, g, c):
                i = target(k, g, c)
                dve.wait_ge(ld_col[c], 16 * (k * GROUPS + g + 1))
                stand(dve, "dve")
                either(dve, summed(k, g, c), lambda: nc.vector.tensor_reduce(
                    part[:, bass.ds(i * R, R // 2), bass.ds(k, 1)].rearrange("p r a -> p (r a)"),
                    col[c][:, 0:R // 2, :], AX.X, ALU.add), None)

            def remainder(k, g, c, half):
                dve.wait_ge(hi_done, 2 * (k * NB + g * VU + c) + half + 1)
                a = (2 * c + half) % 4
                nc.vector.tensor_tensor(lo[a][:], tp[half][:], hi[a][:].bitcast(F32), ALU.subtract).then_inc(lo_done, 1)

            def combine(i):
                c = i % 2
                dve.wait_ge(back_done, i + 1)
                if i >= 2:
                    dve.wait_ge(o_ok, i - 1)
                for r in range(R):
                    t = i * R + r
                    ins = nc.vector.scalar_tensor_tensor(
                        out=y[c][:, r, :], in0=support[:, t, :], scalar=dinv[:, t:t + 1],
                        in1=pre[c][:, r * D:(r + 1) * D], op0=ALU.mult, op1=ALU.add)
                ins.then_inc(t_ok, 1)

            dve.wait_ge(row_done, NB)
            add_totals(0)
            scale_support(0, 0)
            remainder(0, 0, 0, 0)
            block_sums(0, 0, 0)
            remainder(0, 0, 0, 1)

            def body(k, par, g, step_end):
                end = is_last(k) and step_end
                for c in range(VU):
                    v = k * NB + g * VU + c
                    step_ends = step_end and not end and c == VU - 1
                    if step_ends:
                        dve.wait_ge(row_done, NB * k + 2 * NB - 1)
                        add_totals(k + 1)
                    if not (end and c == VU - 1):
                        following = later(k, g, c, 1)
                        remainder(*following, 0)
                        if step_ends:
                            scale_support(k + 1, 1 - par)
                        block_sums(*following)
                        remainder(*following, 1)
                    i = target(k, g, c)
                    dve.wait_ge(used, 4 + 2 * v + 2)
                    rows = acc[:, bass.ds(i * G, G)]
                    if is_last(k):
                        nc.vector.tensor_tensor(fin[c % 2][:], prod[c % 2][:], rows, ALU.add).then_inc(fin_ok, 1)
                        if i >= 1:
                            combine(i - 1)
                    else:
                        nc.vector.tensor_tensor(rows, prod[c % 2][:], rows, ALU.add).then_inc(bank_free, 1)

            groups(dve, body)

            combine(NB - 1)


_INS = ['x', 'adj', 'L0_gnn_W']
_OUTS = [((8192, 128), 'float32')]


def kernel(**inputs):
    import numpy as _np
    import concourse.bacc as _bacc
    from concourse import mybir as _mybir
    from concourse.bass_utils import run_bass_kernel_spmd as _run

    nc = _bacc.Bacc("TRN2", target_bir_lowering=False, num_devices=1)
    arrays, args = {}, []
    for name in _INS:
        a = _np.ascontiguousarray(inputs[name])
        arrays[f"in_{name}_dram"] = a
        args.append(nc.dram_tensor(f"in_{name}_dram", a.shape, _mybir.dt.from_np(a.dtype), kind="ExternalInput").ap())
    for i, (shape, dtype) in enumerate(_OUTS):
        dt = _mybir.dt.from_np(_np.dtype(dtype))
        args.append(nc.dram_tensor(f"out_{i}_dram", shape, dt, kind="ExternalOutput").ap())
    gnn_kernel(nc, *args)
    r = _run(nc, [arrays], core_ids=[0])
    got = tuple(r.results[0][f"out_{i}_dram"] for i in range(len(_OUTS)))
    return got[0]
```

```python
import concourse.bass as bass
from concourse import mybir
from contextlib import ExitStack

F32 = mybir.dt.float32
F32R = mybir.dt.float32r
ALU = mybir.AluOpType
ACT = mybir.ActivationFunctionType
AX = mybir.AxisListType


def gnn_kernel(nc: bass.Bass, x: bass.AP, adj: bass.AP, w: bass.AP, out: bass.AP):
    P = 128
    N, D = x.shape
    G = 512
    NB = N // G
    R = G // P
    NT = N // P
    VU = 4
    GROUPS = NB // VU
    KEPT = 2
    STORE_LAG = 5
    LEAD = 1
    XC = 4
    TX = NT // XC
    EPS = 1e-5
    CHAIN_X = 6

    adj_v = adj.rearrange("(i r p) j -> i p r j", r=R, p=P)
    x_v = x.rearrange("(t p) f -> p t f", p=P)
    out_v = out.rearrange("(t p) f -> p t f", p=P)

    ctx = ExitStack()
    with ctx:
        def sb(name, shape, dt=F32):
            return ctx.enter_context(nc.sbuf_tensor(name, shape, dt))

        def pb(name, shape):
            return ctx.enter_context(nc.psum_tensor(name, shape, F32))

        def sem(name):
            return ctx.enter_context(nc.semaphore(name))

        ident = sb("ident", [P, P])
        w_sb = sb("w_sb", [D, D])
        wT = sb("wT", [D, D])
        support = sb("support", [P, NT, D])
        acc = sb("acc", [D, N])
        col = [sb(f"col{i}", [P, R, G]) for i in range(VU)]
        row = [sb(f"row{i}", [P, R, G]) for i in range(VU)]
        hi = [sb(f"hi{i}", [P, 2 * G], F32R) for i in range(4)]
        lo = [sb(f"lo{i}", [P, 2 * G], F32R) for i in range(2)]
        diag = sb("diag", [P, R, G])
        above = [sb(f"above{i}", [P, R, G]) for i in range(2)]
        s_hi = [sb(f"s_hi{i}", [P, R, D], F32R) for i in range(2)]
        s_lo = [sb(f"s_lo{i}", [P, R, D], F32R) for i in range(2)]
        part = sb("part", [P, NT, NB + 1])
        total = sb("total", [P, R])
        power = sb("power", [P, TX])
        empty, dve_empty = sb("empty", [P, VU]), sb("dve_empty", [P, VU])
        root = sb("root", [P, R])
        dinv = sb("dinv", [P, NT])
        stats = sb("stats", [P, NT, 6])
        mean = sb("mean", [P, NT])
        gap = sb("gap", [P, NT])
        var = sb("var", [P, NT])
        rstd = sb("rstd", [P, NT])
        shift = sb("shift", [P, NT])
        h = [sb(f"h{i}", [P, R, D]) for i in range(2)]
        hT = [sb(f"hT{i}", [D, R * P]) for i in range(2)]
        unread = [h[0].rearrange("p r d -> p (r d)"), h[1].rearrange("p r d -> p (r d)"), hT[0], hT[1]]
        side_unread = [[sb(f"side_unread{i}", [P, G])[:] for i in range(2)]]
        fin = [row[0][:, i, :] for i in range(2)]
        y = [row[0][:, 2 + i, :].rearrange("p (r d) -> p r d", d=D) for i in range(2)]
        xin = [row[3][:, i, :].rearrange("p (r d) -> p r d", d=D) for i in range(2)]
        o = [row[3][:, 2 + i, :].rearrange("p (r d) -> p r d", d=D) for i in range(2)]

        tp = [pb(f"tp{i}", [P, 2 * G]) for i in range(2)]
        prod = [pb(f"prod{i}", [P, G]) for i in range(2)]
        pre = [pb(f"pre{i}", [P, G]) for i in range(2)]
        side_unread.append([b[:] for b in pre])
        hT_bank, sup_bank = (pre[0], prod[0]), (pre[1], prod[1])

        ld_w, ident_ok, wT_ps, wT_ok = sem("ld_w"), sem("ident_ok"), sem("wT_ps"), sem("wT_ok")
        ld_x = [sem(f"ld_x{i}") for i in range(XC)]
        ld_col = [sem(f"ld_col{i}") for i in range(VU)]
        ld_diag, ld_above = sem("ld_diag"), [sem(f"ld_above{i}") for i in range(2)]
        ld_row = [sem(f"ld_row{i}") for i in range(VU)]
        stats_chain, stats_ok = sem("stats_chain"), sem("stats_ok")
        var_ok, rstd_ok, total_ok, root_ok = sem("var_ok"), sem("rstd_ok"), sem("total_ok"), sem("root_ok")
        h_ok, hT_ps, hT_ok, sup_ps, sup_ok = sem("h_ok"), sem("hT_ps"), sem("hT_ok"), sem("sup_ps"), sem("sup_ok")
        dve_row_done = sem("dve_row_done")
        row_done = sem("row_done")
        tp_done, hi_done, lo_done = sem("tp_done"), sem("hi_done"), sem("lo_done")
        used = sem("used")
        bank_free = sem("bank_free")
        hi_scaled, s_ready = sem("hi_scaled"), sem("s_ready")
        fin_ok, back_done, t_ok, y_ok, o_ok = sem("fin_ok"), sem("back_done"), sem("t_ok"), sem("y_ok"), sem("o_ok")
        ld_xin = [sem(f"ld_xin{i}") for i in range(2)]
        st_out = [sem(f"st_out{i}") for i in range(2)]

        passed = {e: sem(f"passed_{e}") for e in ("sp", "act", "dve", "pool")}

        block = ctx.enter_context(nc.Block())

        def stand(eng, name):
            eng.sem_inc(passed[name], 1)

        def later(k, par, g, c):
            g, c = g + (c + 1) // VU, (c + 1) % VU
            return (k + 1, 1 - par, 0, c) if isinstance(g, int) and g == GROUPS else (k, par, g, c)

        def is_last(k):
            return isinstance(k, int) and k == NB - 1

        def target(k, g, c):
            s = g * VU + c
            if isinstance(s, int) and s < KEPT:
                return (k - s) & (NB - 1) if isinstance(k, int) else (k + NB - s) & (NB - 1)
            return (k + 1 + s - KEPT) & (NB - 1)

        def within(value, least, most):
            return value if isinstance(value, int) else value.with_bounds(min_val=least, max_val=most)

        def leaving(n):
            return NB - 1 - n if isinstance(n, int) and n < KEPT else n - KEPT

        def either(eng, condition, then, otherwise):
            if isinstance(condition, bool):
                chosen = then if condition else otherwise
                if chosen is not None:
                    chosen()
                return
            with eng.If(condition):
                then()
            if otherwise is not None:
                with eng.Else():
                    otherwise()

        def summed(k, g, c):
            s = g * VU + c
            if is_last(k) or (isinstance(s, int) and s < KEPT):
                return False
            return s < NB - 1 - k + KEPT

        ROWS = NB - 1 - KEPT
        assert all(s * n * 5 >> 6 <= s and (s + 1) * n * 5 // 64 - s * n * 5 // 64 <= 1 and ROWS * n * 5 >> 6 == n
                   for n in range(ROWS + 1) for s in range(ROWS))

        def streamed(k, s):
            return (s * (ROWS - k) * 5) >> 6

        def in_row_stream(k, s):
            if (isinstance(k, int) and k >= ROWS) or (isinstance(s, int) and s >= ROWS):
                return False
            return streamed(k, s) < streamed(k, s + 1)

        def stream_block(k, s):
            return within(k + 1 + KEPT + streamed(k, s), 1 + KEPT, NB - 1)

        def groups(eng, body):
            def step(k, par):
                body(k, par, 0, False)
                with eng.Fori(1, GROUPS - 1) as g:
                    body(k, par, g, False)
                body(k, par, GROUPS - 1, True)

            with eng.Fori(0, NB // 2 - 1) as k2:
                for par in range(2):
                    step(k2 * 2 + par, par)
            step(NB - 2, 0)
            for g in range(GROUPS):
                body(NB - 1, 1, g, g == GROUPS - 1)

        assert KEPT * 2 == VU

        def visited(par, g, c):
            if isinstance(g, int) and g == 0 and c < KEPT:
                return diag if c == 0 else above[1 - par]
            return col[(KEPT * par + c - KEPT) % VU]

        def wait_visited(eng, k, par, g, c):
            if isinstance(g, int) and g == 0 and c < KEPT:
                if c == 0:
                    eng.wait_ge(ld_diag, 16 * (k + 1))
                else:
                    eng.wait_ge(ld_above[1 - par], 8 * (k - par) + 16)
            else:
                before = 16 // VU * (NB - KEPT) * (k - par)
                eng.wait_ge(ld_col[(KEPT * par + c - KEPT) % VU],
                            before + 16 * (g + 1 + ((NB - KEPT) * par + c - KEPT) // VU))

        def first_block(g, c):
            return (diag, above[0])[c] if isinstance(g, int) and g == 0 and c < KEPT else row[c]

        def wait_first(eng, g, c):
            if isinstance(g, int) and g == 0 and c < KEPT:
                eng.wait_ge((ld_diag, ld_above[0])[c], 16)
            else:
                eng.wait_ge(ld_row[c], 16 * (g if c < KEPT else g + 1))

        SIDE = (NB - 3, NB - 2)

        def side_block(k, par, s):
            if not isinstance(s, int) or s not in SIDE or is_last(k) or (s == SIDE[1] and isinstance(k, int) and k == NB - 2):
                return None
            if s == SIDE[0]:
                return diag, k + 1, ld_diag, 16 * (k + 2)
            return above[1 - par], within(k + 2, 2, NB - 1), ld_above[1 - par], 8 * (k - par) + 32

        @block.sync
        def _(sp):
            def load(buffer, i, j, ready):
                sp.dma_start(buffer[:], adj_v[bass.ds(i, 1), :, :, bass.ds(j * G, G)]
                             .rearrange("a p r c -> (a p) r c")).then_inc(ready, 16)

            sp.dma_start(w_sb[:], w).then_inc(ld_w, 16)
            assert XC == VU
            for q in range(XC):
                sp.dma_start(support[:, q * TX:(q + 1) * TX, :], x_v[:, q * TX:(q + 1) * TX, :]).then_inc(ld_x[q], 16)
                if q == 0:
                    load(diag, 0, 0, ld_diag)
                elif q == 1:
                    load(above[0], 0, 1, ld_above[0])
                else:
                    load(row[q], 0, q, ld_row[q])
            for c in range(2):
                load(row[c], 0, VU + c, ld_row[c])
            for c in range(2, VU):
                sp.wait_ge(row_done, c + 1)
                sp.wait_ge(dve_row_done, c + 1)
                load(row[c], 0, VU + c, ld_row[c])
            with sp.Fori(2, GROUPS) as g:
                for c in range(VU):
                    sp.wait_ge(row_done, (g - 1) * VU + c + 1)
                    sp.wait_ge(dve_row_done, (g - 1) * VU + c + 1)
                    stand(sp, "sp")
                    load(row[c], 0, g * VU + c, ld_row[c])
            load(above[1], NB - 1, 0, ld_above[1])

            def column_load(k, par, s):
                if s >= KEPT + VU or not isinstance(k, int) or k > 0:
                    sp.wait_ge(lo_done, 2 * (k * NB + s - VU - (0 if s >= KEPT + VU else KEPT)) + 2)
                    stand(sp, "sp")
                n = (KEPT * par + s - KEPT) % VU
                load(col[n], target(k, *divmod(s, VU)), k, ld_col[n])

            def row_load(k, s):
                c = s % VU
                back = 2 * VU if 0 < s < VU and not (isinstance(k, int) and k == 0) else VU
                sp.wait_ge(dve_row_done, k * NB + s + NB - back + 1)
                sp.wait_ge(row_done, k * NB + s + NB - back + 1)
                stand(sp, "sp")
                either(sp, in_row_stream(k, s),
                       lambda: load(row[c], within(k + 1, 1, NB - 1), stream_block(k, s), ld_row[c]),
                       lambda: sp.sem_inc(ld_row[c], 16))

            def load_xin(n):
                sp.dma_start(xin[n % 2], x_v[:, leaving(n) * R:(leaving(n) + 1) * R, :]).then_inc(ld_xin[n % 2], 16)

            def store(n):
                sp.wait_ge(o_ok, n + 1)
                sp.dma_start(out_v[:, leaving(n) * R:(leaving(n) + 1) * R, :], o[n % 2]).then_inc(st_out[n % 2], 16)
                if n + 2 < NB:
                    load_xin(n + 2)

            def step(k, par):
                for s in range(NB):
                    for s_col in range(KEPT if s == 0 else s + LEAD, min(s + LEAD + 1, NB)):
                        column_load(k, par, s_col)
                    if is_last(k):
                        if s == STORE_LAG - 1:
                            sp.wait_ge(row_done, NB * NB)
                            sp.wait_ge(dve_row_done, NB * NB)
                            load_xin(0)
                            load_xin(1)
                        if s >= STORE_LAG:
                            store(s - STORE_LAG)
                        continue
                    if s == SIDE[0]:
                        load(diag, k + 1, k + 1, ld_diag)
                    if s == SIDE[1] and not (isinstance(k, int) and k == NB - 2):
                        load(above[1 - par], within(k + 1, 1, NB - 2), within(k + 2, 2, NB - 1), ld_above[1 - par])
                    row_load(k, s)

            step(0, 0)
            with sp.Fori(0, NB // 2 - 2) as k2:
                step(k2 * 2 + 1, 1)
                step(k2 * 2 + 2, 0)
            for k in range(NB - 3, NB):
                step(k, k % 2)
            for n in range(NB - STORE_LAG, NB):
                store(n)
            for c in range(2):
                sp.wait_ge(st_out[c], 16 * NB // 2)

        @block.gpsimd
        def _(pool):
            nc.gpsimd.memset(ident[:], 0.0).then_inc(ident_ok, 1)
            pool.wait_ge(ident_ok, 1)
            nc.gpsimd.affine_select(out=ident[:], in_=ident[:], compare_op=ALU.not_equal, fill=1.0, base=0,
                                    pattern=[[-1, P]], channel_multiplier=1).then_inc(ident_ok, 1)
            nc.gpsimd.memset(power[:], -0.5).then_inc(ident_ok, 1)
            nc.gpsimd.memset(part[:, :, NB:], 1.0).then_inc(ident_ok, 1)
            for n in range(2):
                nc.gpsimd.memset(acc[:, n * (N // 2):(n + 1) * (N // 2)], 0.0).then_inc(bank_free, 1)
            pool.wait_ge(ident_ok, 3)
            for q in range(XC):
                pool.wait_ge(var_ok, q + 1)
                ts = slice(q * TX, (q + 1) * TX)
                nc.gpsimd.tensor_tensor(rstd[:, ts], var[:, ts], power[:], ALU.pow).then_inc(rstd_ok, 1)
                pool.wait_ge(rstd_ok, q + 1)
                nc.gpsimd.tensor_tensor(shift[:, ts], mean[:, ts], rstd[:, ts], ALU.mult).then_inc(stats_ok, 1)
            with pool.Fori(0, NB) as k:
                pool.wait_ge(total_ok, k + 1)
                stand(pool, "pool")
                nc.gpsimd.tensor_tensor(root[:], total[:], power[:, :R], ALU.pow).then_inc(root_ok, 1)
            def finish(m, c):
                n = 2 * m + c
                pool.wait_ge(ld_xin[c], 16 * (m + 1))
                if not isinstance(m, int):
                    pool.wait_ge(st_out[c], 16 * m)
                pool.wait_ge(y_ok, n + 1)
                stand(pool, "pool")
                nc.gpsimd.tensor_tensor(o[c], y[c], xin[c], ALU.add).then_inc(o_ok, 1)

            for c in range(2):
                finish(0, c)
            with pool.Fori(1, NB // 2) as m:
                for c in range(2):
                    finish(m, c)

        @block.tensor
        def _(pe):
            pe.sem_inc(used, 4)
            pe.wait_ge(ident_ok, 2)
            pe.wait_ge(ld_w, 16)
            nc.tensor.transpose(prod[0][:, :D], w_sb[:], ident[:]).then_inc(wT_ps, 1)

            def h_transpose(b, c):
                pe.wait_ge(h_ok, R * (b + 1))
                for r in range(R):
                    ins = nc.tensor.transpose(hT_bank[c][:, r * P:(r + 1) * P], h[c][:, r, :], ident[:])
                ins.then_inc(hT_ps, 1)

            def h_product(b, c):
                pe.wait_ge(hT_ok, b + 1)
                for r in range(R):
                    ins = nc.tensor.matmul(sup_bank[c][:, r * D:(r + 1) * D], hT[c][:, r * P:(r + 1) * P], wT[:],
                                           start=True, stop=True)
                ins.then_inc(sup_ps, 1)

            pe.wait_ge(wT_ok, 1)
            h_transpose(0, 0)
            h_transpose(1, 1)
            h_product(0, 0)
            h_transpose(2, 0)
            h_product(1, 1)
            with pe.Fori(1, NB // 2 - 1) as m:
                for c in range(2):
                    b = 2 * m + c
                    h_transpose(b + 1, 1 - c)
                    pe.wait_ge(sup_ok, b - 1)
                    h_product(b, c)
            h_transpose(NB - 1, 1)
            for b in (NB - 2, NB - 1):
                pe.wait_ge(sup_ok, b - 1)
                h_product(b, b % 2)

            def transposes(k, par, g, c, half):
                if half == 0:
                    wait_visited(pe, k, par, g, c)
                for jj in range(2):
                    j = 2 * half + jj
                    for r in range(R):
                        ins = nc.tensor.transpose(tp[half][:, jj * G + r * P:jj * G + (r + 1) * P],
                                                  visited(par, g, c)[:, r, j * P:(j + 1) * P], ident[:])
                ins.then_inc(tp_done, 1)

            def rows_back(n):
                c = n % 2
                pe.wait_ge(fin_ok, n + 1)
                if n >= 2:
                    pe.wait_ge(t_ok, n - 1)
                for r in range(R):
                    ins = nc.tensor.transpose(pre[c][:, r * D:(r + 1) * D], fin[c][:, r * P:(r + 1) * P], ident[:])
                ins.then_inc(back_done, 1)

            pe.wait_ge(row_done, 1)
            transposes(0, 0, 0, 0, 0)
            transposes(0, 0, 0, 0, 1)

            def body(k, par, g, step_end):
                end = is_last(k) and step_end
                for c in range(VU):
                    v = k * NB + g * VU + c
                    for half in range(2):
                        pe.wait_ge(lo_done, 2 * v + half + 1)
                        if not (end and c == VU - 1):
                            transposes(*later(k, par, g, c), half)
                        if half == 0:
                            if is_last(k) and g * VU + c >= 2:
                                pe.wait_ge(fin_ok, g * VU + c - 1)
                            else:
                                pe.wait_ge(bank_free, v + 1)
                        at_hi, at_lo = hi[(2 * c + half) % 4], lo[half]
                        for jj in range(2):
                            j = 2 * half + jj
                            at = slice(jj * G, (jj + 1) * G)
                            if isinstance(g, int) and g == 0 and c == 0:
                                pe.wait_ge(s_ready, k * R + j + 1)
                            for n, (s, m) in enumerate(((s_hi, at_hi), (s_lo, at_hi), (s_hi, at_lo))):
                                ins = nc.tensor.matmul(prod[c % 2][:], s[par][:, j, :], m[:, at],
                                                       start=(j == 0 and n == 0), stop=(j == R - 1 and n == 2))
                        ins.then_inc(used, 1)
                        if is_last(k) and half == 0 and v > NB * (NB - 1):
                            rows_back(g * VU + c - 1)

            groups(pe, body)

            rows_back(NB - 1)

        @block.scalar
        def _(act):
            def row_sums(i, j, block):
                for r in range(1, R):
                    ins = nc.scalar.activation(block[:, r, :], block[:, r, :], ACT.Copy,
                                               accum_out=part[:, bass.ds(i * R + r, 1), bass.ds(j, 1)]
                                               .rearrange("p a b -> p (a b)"))
                return ins

            def layernorm(b, c):
                act.wait_ge(stats_ok, b // (TX // R) + 1)
                for r in range(R):
                    t = b * R + r
                    nc.scalar.activation(h[c][:, r, :], support[:, bass.ds(t, 1), :].rearrange("p a f -> p (a f)"),
                                         ACT.Relu, bias=shift[:, bass.ds(t, 1)],
                                         scale=rstd[:, bass.ds(t, 1)]).then_inc(h_ok, 1)

            def first_sums(g, c):
                wait_first(act, g, c)
                block = first_block(g, c)
                for r in range(R // 2, R):
                    ins = nc.scalar.activation(block[:, r, :], block[:, r, :], ACT.Copy,
                                               accum_out=part[:, r, bass.ds(g * VU + c, 1)])
                ins.then_inc(row_done, 1)

            first_sums(0, 0)
            first_sums(0, 1)
            layernorm(0, 0)
            first_sums(0, 2)
            layernorm(1, 1)
            first_sums(0, 3)
            with act.Fori(1, GROUPS) as g:
                for c in range(VU):
                    b = g * VU + c - 2
                    act.wait_ge(hT_ps, b - 1)
                    layernorm(b, c % 2)
                    first_sums(g, c)
            for b in range(NB - 2, NB):
                act.wait_ge(hT_ps, b - 1)
                layernorm(b, b % 2)

            def late_half_sums(block, i, j, to):
                for r in range(R // 2, R):
                    nc.scalar.activation(to[r - R // 2], block[:, r, :], ACT.Copy,
                                         accum_out=part[:, bass.ds(i * R + r, 1), bass.ds(j, 1)]
                                         .rearrange("p a b -> p (a b)"))

            def block_sums(k, par, g, c):
                i = target(k, g, c)
                wait_visited(act, k, par, g, c)
                stand(act, "act")
                either(act, summed(k, g, c), lambda: late_half_sums(
                    visited(par, g, c), i, k, [unread[c % 2 * 2][:], unread[c % 2 * 2 + 1][:]]), None)

            def relu(n):
                act.wait_ge(t_ok, n + 1)
                for r in range(R):
                    t = leaving(n) * R + r
                    ins = nc.scalar.activation(y[n % 2][:, r, :], y[n % 2][:, r, :], ACT.Relu,
                                               scale=dinv[:, t:t + 1])
                ins.then_inc(y_ok, 1)

            act.wait_ge(sup_ps, NB)

            def body(k, par, g, step_end):
                for c in range(VU):
                    s = g * VU + c
                    v = k * NB + s
                    for half in range(2):
                        q = 2 * v + half
                        act.wait_ge(used, q + 1)
                        act.wait_ge(tp_done, q + 1)
                        nc.scalar.activation(hi[(2 * c + half) % 4][:], tp[half][:], ACT.Copy).then_inc(hi_done, 1)
                        if half == 0:
                            block_sums(k, par, g, c)
                    if is_last(k):
                        if s >= 3:
                            relu(s - 3)
                        continue
                    side = side_block(k, par, s)
                    if side is not None:
                        block, j, ready, count = side
                        act.wait_ge(ready, count)
                        stand(act, "act")
                    act.wait_ge(ld_row[c], 16 * (GROUPS * (k + 1) + g + 1 - (c < KEPT)))
                    stand(act, "act")
                    if side is not None:
                        late_half_sums(block, k + 1, j, side_unread[s % 2])
                    either(act, in_row_stream(k, s),
                           lambda: row_sums(within(k + 1, 1, NB - 1), stream_block(k, s), row[c])
                           .then_inc(row_done, 1),
                           lambda: nc.scalar.activation(empty[:, c:c + 1], power[:, 0:1], ACT.Copy)
                           .then_inc(row_done, 1))

            groups(act, body)

            for i in range(NB - 3, NB):
                relu(i)

        @block.vector
        def _(dve):
            dve.wait_ge(wT_ps, 1)
            nc.vector.tensor_copy(wT[:], prod[0][:, :D]).then_inc(wT_ok, 1)

            def row_statistics(q, quarter):
                dve.wait_ge(ld_x[q], 16)
                first = q * TX + quarter * (TX // 4)
                for t in range(first, first + TX // 4):
                    ins = nc.vector.bn_stats(stats[:, t, :], support[:, t, :])
                if quarter == 3:
                    ins.then_inc(stats_chain, 1)

            def statistics(q):
                ts = slice(q * TX, (q + 1) * TX)
                done = q * CHAIN_X
                dve.wait_ge(stats_chain, done + 1)
                even, odd = stats[:, ts, 0:3], stats[:, ts, 3:6]
                nc.vector.tensor_tensor(mean[:, ts], even[:, :, 1], odd[:, :, 1], ALU.add).then_inc(stats_chain, 1)
                nc.vector.tensor_tensor(gap[:, ts], even[:, :, 1], odd[:, :, 1], ALU.subtract).then_inc(stats_chain, 1)
                nc.vector.tensor_tensor(var[:, ts], even[:, :, 2], odd[:, :, 2], ALU.add).then_inc(stats_chain, 1)
                dve.wait_ge(stats_chain, done + 3)
                nc.vector.tensor_scalar(mean[:, ts], mean[:, ts], -0.5, None, ALU.mult)
                nc.vector.scalar_tensor_tensor(out=gap[:, ts], in0=gap[:, ts], scalar=D / 4, in1=gap[:, ts],
                                               op0=ALU.mult, op1=ALU.mult).then_inc(stats_chain, 1)
                dve.wait_ge(stats_chain, done + 5)
                nc.vector.tensor_tensor(var[:, ts], var[:, ts], gap[:, ts], ALU.add).then_inc(stats_chain, 1)
                dve.wait_ge(stats_chain, done + CHAIN_X)
                nc.vector.tensor_scalar(var[:, ts], var[:, ts], 1 / D, EPS, ALU.mult, ALU.add).then_inc(var_ok, 1)

            def hT_out(b):
                dve.wait_ge(hT_ps, b + 1)
                nc.vector.tensor_copy(hT[b % 2][:], hT_bank[b % 2][:]).then_inc(hT_ok, 1)

            def support_out(b):
                dve.wait_ge(sup_ps, b + 1)
                nc.vector.tensor_copy(support[:, b * R:(b + 1) * R, :].rearrange("p a f -> p (a f)"),
                                      sup_bank[b % 2][:]).then_inc(sup_ok, 1)

            def first_sums(b):
                wait_first(dve, b // VU, b % VU)
                nc.vector.tensor_reduce(part[:, 0:R // 2, b], first_block(b // VU, b % VU)[:, 0:R // 2, :],
                                        AX.X, ALU.add).then_inc(dve_row_done, 1)

            for quarter in range(4):
                row_statistics(0, quarter)
            statistics(0)
            first_sums(0)
            first_sums(1)
            for quarter in range(4):
                row_statistics(1, quarter)
            statistics(1)
            for b in range(NB):
                hT_out(b)
                if b > 0:
                    support_out(b - 1)
                if b + 2 < NB:
                    first_sums(b + 2)
                if b < 8:
                    row_statistics(2 + b // 4, b % 4)
                if b in (3, 7):
                    statistics(2 + b // 4)
            support_out(NB - 1)

            def add_totals(i):
                nc.vector.tensor_reduce(total[:], part[:, bass.ds(i * R, R), :], AX.X, ALU.add).then_inc(total_ok, 1)

            def scale_support(i, par):
                dve.wait_ge(root_ok, i + 1)

                def tile(r):
                    return support[:, bass.ds(i * R + r, 1), :].rearrange("p a f -> p (a f)")

                for pair in range(0, R, 2):
                    for r in (pair, pair + 1):
                        nc.vector.tensor_scalar(s_hi[par][:, r, :], tile(r), root[:, r:r + 1], None,
                                                ALU.mult).then_inc(hi_scaled, 1)
                    for r in (pair, pair + 1):
                        dve.wait_ge(hi_scaled, i * R + r + 1)
                        nc.vector.scalar_tensor_tensor(out=s_lo[par][:, r, :], in0=tile(r), scalar=root[:, r:r + 1],
                                                       in1=s_hi[par][:, r, :].bitcast(F32),
                                                       op0=ALU.mult, op1=ALU.subtract).then_inc(s_ready, 1)
                nc.vector.tensor_copy(dinv[:, bass.ds(i * R, R)], root[:])

            def early_half_sums(block, i, j):
                nc.vector.tensor_reduce(part[:, bass.ds(i * R, R // 2), bass.ds(j, 1)].rearrange("p r a -> p (r a)"),
                                        block[:, 0:R // 2, :], AX.X, ALU.add)

            def block_sums(k, par, g, c):
                i = target(k, g, c)
                wait_visited(dve, k, par, g, c)
                stand(dve, "dve")
                either(dve, summed(k, g, c), lambda: early_half_sums(visited(par, g, c), i, k), None)

            def remainder(k, par, g, c, half):
                q = 2 * (k * NB + g * VU + c) + half
                dve.wait_ge(used, q + 3)
                dve.wait_ge(hi_done, q + 1)
                nc.vector.tensor_tensor(lo[half][:], tp[half][:], hi[(2 * c + half) % 4][:].bitcast(F32),
                                        ALU.subtract).then_inc(lo_done, 1)

            def combine(n):
                c = n % 2
                dve.wait_ge(back_done, n + 1)
                if n >= 2:
                    dve.wait_ge(o_ok, n - 1)
                for r in range(R):
                    t = leaving(n) * R + r
                    ins = nc.vector.scalar_tensor_tensor(
                        out=y[c][:, r, :], in0=support[:, t, :], scalar=dinv[:, t:t + 1],
                        in1=pre[c][:, r * D:(r + 1) * D], op0=ALU.mult, op1=ALU.add)
                ins.then_inc(t_ok, 1)

            def row_sums(k, g, c):
                dve.wait_ge(ld_row[c], 16 * (GROUPS * (k + 1) + g + 1 - (c < KEPT)))
                stand(dve, "dve")
                either(dve, in_row_stream(k, g * VU + c),
                       lambda: nc.vector.tensor_reduce(
                           part[:, bass.ds((k + 1) * R, 1), bass.ds(stream_block(k, g * VU + c), 1)]
                           .rearrange("p r a -> p (r a)"), row[c][:, 0:1, :], AX.X, ALU.add)
                       .then_inc(dve_row_done, 1),
                       lambda: nc.vector.tensor_copy(dve_empty[:, c:c + 1], power[:, 0:1])
                       .then_inc(dve_row_done, 1))

            dve.wait_ge(ident_ok, 4)
            dve.wait_ge(row_done, NB)
            dve.wait_ge(dve_row_done, NB)
            add_totals(0)
            scale_support(0, 0)
            remainder(0, 0, 0, 0, 0)
            remainder(0, 0, 0, 0, 1)
            dve.wait_ge(ld_above[1], 16)
            nc.vector.tensor_reduce(part[:, (NB - 1) * R:NB * R, 0], above[1][:], AX.X, ALU.add)

            def body(k, par, g, step_end):
                end = is_last(k) and step_end
                for c in range(VU):
                    v = k * NB + g * VU + c
                    step_ends = step_end and not end and c == VU - 1
                    if step_ends:
                        dve.wait_ge(row_done, NB * k + 2 * NB - 1)
                        dve.wait_ge(lo_done, 2 * v + 2)
                        add_totals(k + 1)
                    if not (end and c == VU - 1):
                        following = later(k, par, g, c)
                        remainder(*following, 0)
                        if step_ends:
                            scale_support(k + 1, 1 - par)
                        block_sums(*following)
                        side = side_block(k, par, g * VU + c)
                        if side is not None:
                            block, j, ready, count = side
                            dve.wait_ge(ready, count)
                            early_half_sums(block, k + 1, j)
                        remainder(*following, 1)
                        if not is_last(k):
                            row_sums(k, g, c)
                    i = target(k, g, c)
                    dve.wait_ge(used, 4 + 2 * v + 2)
                    rows = acc[:, bass.ds(i * G, G)]
                    if is_last(k):
                        if g == 0 and c == 0:
                            dve.wait_ge(row_done, NB * NB)
                        nc.vector.tensor_tensor(fin[c % 2], prod[c % 2][:], rows, ALU.add).then_inc(fin_ok, 1)
                        if g * VU + c >= 1:
                            combine(g * VU + c - 1)
                    else:
                        nc.vector.tensor_tensor(rows, prod[c % 2][:], rows, ALU.add).then_inc(bank_free, 1)

            groups(dve, body)

            combine(NB - 1)


_INS = ['x', 'adj', 'L0_gnn_W']
_OUTS = [((8192, 128), 'float32')]


def kernel(**inputs):
    import numpy as _np
    import concourse.bacc as _bacc
    from concourse import mybir as _mybir
    from concourse.bass_utils import run_bass_kernel_spmd as _run

    nc = _bacc.Bacc("TRN2", target_bir_lowering=False, num_devices=1)
    arrays, args = {}, []
    for name in _INS:
        a = _np.ascontiguousarray(inputs[name])
        arrays[f"in_{name}_dram"] = a
        args.append(nc.dram_tensor(f"in_{name}_dram", a.shape, _mybir.dt.from_np(a.dtype), kind="ExternalInput").ap())
    for i, (shape, dtype) in enumerate(_OUTS):
        dt = _mybir.dt.from_np(_np.dtype(dtype))
        args.append(nc.dram_tensor(f"out_{i}_dram", shape, dt, kind="ExternalOutput").ap())
    gnn_kernel(nc, *args)
    r = _run(nc, [arrays], core_ids=[0])
    got = tuple(r.results[0][f"out_{i}_dram"] for i in range(len(_OUTS)))
    return got[0]
```
